# Optimizing a Trainium2 kernel written in Bass

```python
import numpy as np
import jax
import jax.numpy as jnp

def _softmax(x, axis=-1):
    return jax.nn.softmax(x, axis=axis)

def _gelu(x):
    return jax.nn.gelu(x, approximate=True)

def _silu(x):
    return jax.nn.silu(x)

def _sigmoid(x):
    return jax.nn.sigmoid(x)

def _layernorm(x, axis=-1, eps=1e-05):
    m = jnp.mean(x, axis=axis, keepdims=True)
    v = jnp.var(x, axis=axis, keepdims=True)
    return (x - m) / jnp.sqrt(v + eps)

def _scatter_add(tgt, idx, src, axis=0):
    return tgt.at[idx].add(src)

def _segment_sum(src, seg, n):
    return jax.ops.segment_sum(src, seg, n)
kernel_name = 'mk_xattn_ffn_d1_seqx_r4_75c39f'

def setup_inputs(seed: int=0):
    np.random.seed(seed)
    _w = jnp.asarray

    def _rec_inputs():
        import jax
        import jax.numpy as jnp
        _rk = jax.random.key(seed)
        x = -0.000125 + 0.9999 * jax.random.normal(jax.random.fold_in(_rk, 1), (8, 256, 512), jnp.float32)
        _lenS = 256 - jax.random.randint(jax.random.fold_in(_rk, 7), (8,), 0, max(1, 256 // 4) + 1, jnp.int32)
        _lenS2 = 256 - jax.random.randint(jax.random.fold_in(_rk, 8), (8,), 0, max(1, 256 // 4) + 1, jnp.int32)
        _ctx_2048P = jax.random.normal(jax.random.fold_in(_rk, 11), (8, 16, 512), jnp.float32)
        _ctx_2048c = jax.random.dirichlet(jax.random.fold_in(_rk, 511), 0.3 * jnp.ones((16,), jnp.float32), (8, 256))
        _ctx_2048t = jnp.einsum('bsk,bkd->bsd', _ctx_2048c, _ctx_2048P)
        _ctx_2048t = _ctx_2048t * jax.lax.rsqrt(jnp.mean(jnp.square(_ctx_2048t)) + 1e-12) * 0.953939
        ctx_2048 = -1.52775e-05 + 0.999936 * (_ctx_2048t + 0.3 * jax.random.normal(jax.random.fold_in(_rk, 611), (8, 256, 512), jnp.float32))
        return (x, ctx_2048)
    x, ctx_2048 = _rec_inputs()

    def _L0_xattn_setup():
        import jax, jax.numpy as jnp
        import numpy as np
        B, DIM1, DIM2, LATENT, T = (16, 256, 256, 128, 512)
        LN_EPS = 1e-05
        key = jax.random.key(seed)
        ks = jax.random.split(key, 8)

        def xavier(k, shape):
            fan_out, fan_in = shape
            std = float(np.sqrt(2.0 / (fan_in + fan_out)))
            return jax.random.normal(k, shape, dtype=jnp.float32) * std
        return {'input1': jax.random.normal(ks[0], (B, DIM1, T), dtype=jnp.float32), 'input2': jax.random.normal(ks[1], (B, DIM2, T), dtype=jnp.float32), 'theta_w': xavier(ks[2], (LATENT, DIM2)), 'theta_b': jnp.zeros((LATENT,), jnp.float32), 'phi_w': xavier(ks[3], (LATENT, DIM1)), 'phi_b': jnp.zeros((LATENT,), jnp.float32), 'g_w': xavier(ks[4], (LATENT, DIM1)), 'g_b': jnp.zeros((LATENT,), jnp.float32), 'ln_gamma': jnp.ones((LATENT, T), jnp.float32), 'ln_beta': jnp.zeros((LATENT, T), jnp.float32), 'out_w': xavier(ks[5], (DIM2, LATENT)), 'out_b': jnp.zeros((DIM2,), jnp.float32)}
    _L0_xattn_all = _L0_xattn_setup()
    _L0_xattn_in = {k: v for k, v in _L0_xattn_all.items() if k in ('theta_w', 'theta_b', 'phi_w', 'phi_b', 'g_w', 'g_b', 'ln_gamma', 'ln_beta', 'out_w', 'out_b')}
    del _L0_xattn_all

    def _L0_ffn_setup():
        import jax, jax.numpy as jnp
        import numpy as np
        TOP_K = 8
        NORM_TOPK_PROB = True
        key = jax.random.key(seed)
        k1, k2, k3, k4, k5 = jax.random.split(key, 5)
        B, S, H, E, I = (2, 512, 512, 32, 192)
        scale = 0.02
        return {'x': jax.random.normal(k1, (B, S, H), dtype=jnp.float32), 'gate_w': jax.random.normal(k2, (E, H), dtype=jnp.float32) * scale, 'w_gate': jax.random.normal(k3, (E, H, I), dtype=jnp.float32) * scale, 'w_up': jax.random.normal(k4, (E, H, I), dtype=jnp.float32) * scale, 'w_down': jax.random.normal(k5, (E, I, H), dtype=jnp.float32) * scale}
    _L0_ffn_all = _L0_ffn_setup()
    _L0_ffn_in = {k: v for k, v in _L0_ffn_all.items() if k in ('gate_w', 'w_gate', 'w_up', 'w_down')}
    del _L0_ffn_all
    return {'x': x, 'ctx_2048': ctx_2048, 'L0_xattn_theta_w': _L0_xattn_in['theta_w'], 'L0_xattn_theta_b': _L0_xattn_in['theta_b'], 'L0_xattn_phi_w': _L0_xattn_in['phi_w'], 'L0_xattn_phi_b': _L0_xattn_in['phi_b'], 'L0_xattn_g_w': _L0_xattn_in['g_w'], 'L0_xattn_g_b': _L0_xattn_in['g_b'], 'L0_xattn_ln_gamma': _L0_xattn_in['ln_gamma'], 'L0_xattn_ln_beta': _L0_xattn_in['ln_beta'], 'L0_xattn_out_w': _L0_xattn_in['out_w'], 'L0_xattn_out_b': _L0_xattn_in['out_b'], 'L0_ffn_gate_w': _L0_ffn_in['gate_w'], 'L0_ffn_w_gate': _L0_ffn_in['w_gate'], 'L0_ffn_w_up': _L0_ffn_in['w_up'], 'L0_ffn_w_down': _L0_ffn_in['w_down']}

def reference(x, ctx_2048, L0_xattn_theta_w, L0_xattn_theta_b, L0_xattn_phi_w, L0_xattn_phi_b, L0_xattn_g_w, L0_xattn_g_b, L0_xattn_ln_gamma, L0_xattn_ln_beta, L0_xattn_out_w, L0_xattn_out_b, L0_ffn_gate_w, L0_ffn_w_gate, L0_ffn_w_up, L0_ffn_w_down):
    import jax
    import jax.numpy as jnp

    def _L0_xattn_ref(input1, input2, theta_w, theta_b, phi_w, phi_b, g_w, g_b, ln_gamma, ln_beta, out_w, out_b):
        import jax, jax.numpy as jnp
        import numpy as np
        B, DIM1, DIM2, LATENT, T = (16, 256, 256, 128, 512)
        LN_EPS = 1e-05
        theta_x = jnp.einsum('ld,bdt->btl', theta_w, input2) + theta_b
        phi_x = jnp.einsum('ld,bdt->blt', phi_w, input1) + phi_b[:, None]
        scores = jnp.einsum('btl,bls->bts', theta_x, phi_x)
        p = jax.nn.softmax(scores, axis=-1)
        g_x = jnp.einsum('ld,bdt->btl', g_w, input1) + g_b
        t_x = jnp.einsum('bts,bsl->blt', p, g_x)
        mu = jnp.mean(t_x, axis=(1, 2), keepdims=True)
        var = jnp.var(t_x, axis=(1, 2), keepdims=True)
        h = (t_x - mu) * jax.lax.rsqrt(var + LN_EPS) * ln_gamma + ln_beta
        h = jax.nn.relu(h)
        w_t = jnp.einsum('ol,blt->bot', out_w, h) + out_b[None, :, None]
        return w_t + input2

    def _L0_ffn_ref(x, gate_w, w_gate, w_up, w_down):
        import jax, jax.numpy as jnp
        import numpy as np
        TOP_K = 8
        NORM_TOPK_PROB = True
        B, S, H = x.shape
        E = gate_w.shape[0]
        xt = x.reshape(-1, H)
        T = xt.shape[0]
        router_logits = xt @ gate_w.T
        routing_weights = jax.nn.softmax(router_logits.astype(jnp.float32), axis=-1)
        top_w, top_idx = jax.lax.top_k(routing_weights, TOP_K)
        rows = jnp.arange(T)[:, None]
        full_w = jnp.zeros_like(routing_weights).at[rows, top_idx].set(top_w)
        if NORM_TOPK_PROB:
            denom = jnp.clip(full_w.sum(axis=-1, keepdims=True), 1e-09, None)
            full_w = full_w / denom
        full_w = full_w.astype(x.dtype)
        g = jax.nn.silu(jnp.einsum('th,ehi->eti', xt, w_gate))
        u = jnp.einsum('th,ehi->eti', xt, w_up)
        y = jnp.einsum('eti,eih->eth', g * u, w_down)
        out = jnp.einsum('eth,te->th', y, full_w)
        return out.reshape(B, S, H)
    x = x + _L0_xattn_ref(_layernorm(x, axis=-1), ctx_2048, L0_xattn_theta_w, L0_xattn_theta_b, L0_xattn_phi_w, L0_xattn_phi_b, L0_xattn_g_w, L0_xattn_g_b, L0_xattn_ln_gamma, L0_xattn_ln_beta, L0_xattn_out_w, L0_xattn_out_b)
    x = x + _L0_ffn_ref(_layernorm(x, axis=-1), L0_ffn_gate_w, L0_ffn_w_gate, L0_ffn_w_up, L0_ffn_w_down)
    return x

_drawn_inputs = setup_inputs


def setup_inputs(seed=0):
    import zlib

    import numpy as np

    out = dict(_drawn_inputs(seed))
    spreads = {'L0_xattn_theta_b': (0.0, 0.1),
     'L0_xattn_phi_b': (0.0, 2.0),
     'L0_xattn_g_b': (0.0, 0.1),
     'L0_xattn_ln_gamma': (1.0, 0.2),
     'L0_xattn_ln_beta': (0.0, 0.1),
     'L0_xattn_out_b': (0.0, 0.8)}
    factors = {'L0_ffn_gate_w': 8.0, 'L0_ffn_w_gate': 7.726, 'L0_ffn_w_up': 7.581, 'L0_ffn_w_down': 7.555}
    for name, (base, spread) in spreads.items():
        noise = np.random.default_rng([zlib.crc32(name.encode()), seed]).standard_normal(out[name].shape)
        drawn = base * np.exp(spread * noise) if base else spread * noise
        out[name] = jnp.asarray(drawn.astype(out[name].dtype))
    for name, factor in factors.items():
        out[name] = (out[name] * factor).astype(out[name].dtype)
    return out
```

```python
from contextlib import ExitStack

import concourse.bass as bass
from concourse import mybir

F32 = mybir.dt.float32
ALU = mybir.AluOpType
ACT = mybir.ActivationFunctionType
AX_X = mybir.AxisListType.X
P = 128
EPS = 1e-5
TOPK = 8
LOWEST = -3.0e38
F32R = mybir.dt.float32r
BF16 = mybir.dt.bfloat16
I32 = mybir.dt.int32


def build(nc, x, ctx2, theta_w, theta_b, phi_w, phi_b, g_w, g_b, gamma, beta, out_w, out_b,
          gate_w, w_gate, w_up, w_down, out):
    NB, D, T = x.shape
    L = theta_w.shape[0]
    E, H, I = w_gate.shape
    U = D // P
    NG = NB * U
    TC = T // P
    HC = H // P
    I2 = I - P
    assert L == P and H == T
    TOK = NB * D
    REGION = TOK + P
    NT = TOK * TOPK // P + E
    SPARE = E * REGION
    WCOLS = HC * 2 * I + 2 * H
    GU_END, DA_END = HC * 2 * I, HC * 2 * I + H

    x_v = x.rearrange("b (u p) t -> p (b u) t", p=P)
    ctx_v = ctx2.rearrange("b (u p) t -> p (b u) t", p=P)
    out_v = out.rearrange("b (u p) t -> p (b u) t", p=P)

    with ExitStack() as es:
        def sb(name, shape, dt=F32):
            return es.enter_context(nc.sbuf_tensor(name, shape, dt))

        def sem(name):
            return es.enter_context(nc.semaphore(name))

        bank = [es.enter_context(nc.psum_tensor(f"bank{i}", [P, 512], F32)) for i in range(8)]
        THETA, PHI, GPROJ, ATT = 4, 5, 6, 7

        x_all = sb("x_all", [P, NG, T])
        ctx_all = sb("ctx_all", [P, NG, T])
        xnTb = sb("xnTb", [P, U, HC, P])
        wk_all = sb("wk_all", [P, NG, TOPK])
        slots_all = sb("slots_all", [P, NG, TOPK], I32)
        ident = sb("ident", [P, P])
        mean_mat = sb("mean_mat", [P, P])
        projT = sb("projT", [P, 3, U, L])
        outT = sb("outT", [P, D])
        gateT = sb("gateT", [P, HC, E])
        th_b = sb("th_b", [P, 1])
        ph_b = sb("ph_b", [P, 1])
        gb_row = sb("gb_row", [P, L])
        o_b = sb("o_b", [P, U])
        gam = sb("gam", [P, T])
        bet = sb("bet", [P, T])
        eps = sb("eps", [P, 1])
        xn1 = sb("xn1", [P, U, T])
        bn1 = sb("bn1", [P, U, 6])
        mv1 = sb("mv1", [P, U, 2])
        rstd1 = sb("rstd1", [P, U])
        thX = sb("thX", [P, T])
        phX = sb("phX", [P, T])
        gX = sb("gX", [P, TC, L])
        nmax = sb("nmax", [P, TC])
        esum = sb("esum", [P, TC])
        erec = sb("erec", [P, TC])
        prob = sb("prob", [P, TC, T])
        probT = sb("probT", [P, TC, T])
        raw_proj = probT[:, 0:2, :].rearrange("p a t -> p (a t)")[:, 0:3 * D].rearrange("p (k d) -> p k d", k=3)
        raw_out = probT[:, 2, 0:U * L].rearrange("p (u l) -> p u l", u=U)
        raw_gate = probT[0:E, 3, :]
        xg = prob[:, 0:2, :]
        y_sb = prob[:, 2:4, :]
        sil = probT[:, 0:2, 0:I]
        act = probT[:, 2:4, 0:I]
        bnO = sb("bnO", [P, 6])
        mvO = sb("mvO", [P, 2])
        mu = sb("mu", [P, 1])
        dmu = sb("dmu", [P, 1])
        vO = sb("vO", [P, 1])
        rstdh = sb("rstdh", [P, 1])
        hA = sb("hA", [P, T])
        hB = sb("hB", [P, T])
        hR = sb("hR", [P, T])
        bn2 = sb("bn2", [P, U, 6])
        mv2 = sb("mv2", [P, U, 2])
        rstd2 = sb("rstd2", [P, U])
        xn2 = sb("xn2", [P, U, T])
        top8 = sb("top8", [P, U, 8])
        zl = sb("zl", [P, U, E])
        ez = sb("ez", [P, U, E])
        repl = sb("repl", [P, U, E])
        mask = sb("mask", [P, U, E], BF16)
        mask_sum = sb("mask_sum", [P, E], BF16)
        tri = sb("tri", [P, P], BF16)
        tri_incl = sb("tri_incl", [E, E], BF16)
        ones_b = sb("ones_b", [P, P], BF16)
        rowbase_i = sb("rowbase_i", [P, E], I32)
        rowbase = sb("rowbase", [P, E])
        lane_i = sb("lane_i", [P, 1], I32)
        lane = sb("lane", [P, 1])
        tile_no_i = sb("tile_no_i", [E, NT], I32)
        tile_no = sb("tile_no", [E, NT])
        neg_half = sb("neg_half", [P, U])
        var1 = sb("var1", [P, U])
        varh = sb("varh", [P, 1])
        var2 = sb("var2", [P, U])
        key0 = sb("key0", [P, U, E])
        key = sb("key", [P, U, E])
        key_all = sb("key_all", [P, NG, E])
        n_tile_b = sb("n_tile_b", [E, P], BF16)
        delta = sb("delta", [P, E])
        y_key8 = sb("y_key8", [P, NG, TOPK])
        key8 = sb("key8", [P, U, TOPK])
        slots = sb("slots", [P, U, TOPK], I32)
        hit = sb("hit", [P, U, TOPK, E])
        hit_w = sb("hit_w", [P, U, TOPK, E])
        wk = sb("wk", [P, U, TOPK])
        wsum = sb("wsum", [P, U])
        wrec = sb("wrec", [P, U])
        zero_rows = sb("zero_rows", [P, H])
        pad_slot = sb("pad_slot", [P, E], I32)
        pad_now = [sb(f"pad_now{i}", [P, 1], I32) for i in range(2)]
        n_col = sb("n_col", [E, 1])
        n_cmp = sb("n_cmp", [E, TOK // P])
        n_tile0 = sb("n_tile0", [E, 1])
        n_tile = sb("n_tile", [E, 1], BF16)
        cum_col = sb("cum_col", [E, 1])
        cum_row = sb("cum_row", [1, E], I32)
        past = sb("past", [E, NT], BF16)
        owner = sb("owner", [1, NT])
        owner_row = sb("owner_row", [1, NT])
        tile_in = sb("tile_in", [1, NT])
        row_f = sb("row_f", [1, NT])
        x_row = sb("x_row", [1, NT], I32)
        expert_of = sb("expert_of", [1, NT], I32)
        half_of = sb("half_of", [1, NT], I32)
        w_raw = sb("w_raw", [P, 2, WCOLS])
        w_hi = sb("w_hi", [P, 2, WCOLS], F32R)
        w_lo = sb("w_lo", [P, 2, WCOLS], F32R)
        xT_hi = sb("xT_hi", [P, 2, H], F32R)
        xT_lo = sb("xT_lo", [P, 2, H], F32R)
        aA_hi = sb("aA_hi", [P, 2, P], F32R)
        aA_lo = sb("aA_lo", [P, 2, P], F32R)
        aB = sb("aB", [P, 2, P], F32R)
        x_sorted = nc.dram_tensor("x_sorted", [SPARE + P, H], F32, kind="Internal").ap()
        y_sorted = nc.dram_tensor("y_sorted", [NT * P, H], F32, kind="Internal").ap()
        y_got = ctx_all[:].rearrange("p (s k) h -> p s k h", s=2)

        names = """batch_loaded proj_loaded outw_loaded gatew_loaded vec_loaded const_zero const_ready
        wT_done wT_ready bn1_done mv1_ready rstd1_ready xn1_ready xc_ready
        theta_done phi_done g_done theta_ready phi_ready gx_ready scores_done rowmax_ready exp_ready
        erec_ready pn_ready pt_done pt_act pt_dve pv_done bnO_done bnO_ready mm1_done mu_ready dmu_ready v_ready
        mm2_done rstdh_ready hA_ready hB_ready h_ready outp_done x2_done bn2_done mv2_ready
        rstd2_ready xn2_ready xnT_done xnT_ready logits_done top8_ready zl_ready ez_ready
        repl_ready mask_ready
        pos_done mask0_added mask_sum_ready key0_ready key_ready key8_ready slots_ready hit_ready hit_w_ready wk_ready
        wsum_ready wrec_ready w_ready scattered spare_zeroed
        var1_ready varh_ready var2_ready consts_i consts_f
        count_done n_col_ready n_cmp_ready n_tile0_ready n_tile_ready cum_done cum_ready past_ready owner_done
        owner_ready row_f_ready tables_ready
        pad_copied pad_zeroed hi_split expert_ready gu_done xT_done xT_hi_ready xT_lo_ready sil_ready act_ready
        actT_done aT_hi_ready aT_lo_ready aB_hi_ready y_done y_evac
        dve_passed pool_passed sp_passed combined out_stored before_done delta_ready y_key_ready y_key8_ready y_slots_ready""".split()
        S = {n: sem(n) for n in names}
        raw_loaded = [sem("raw_loaded0"), sem("raw_loaded1")]
        xg_loaded = [sem("xg_loaded0"), sem("xg_loaded1")]
        y_stored = [sem("y_stored0"), sem("y_stored1")]
        y_got_loaded = [sem("y_got_loaded0"), sem("y_got_loaded1")]
        block = es.enter_context(nc.Block())

        def wait(eng, name, value):
            if type(value) is not int or value > 0:
                eng.wait_ge(S[name], value)

        def wait_apart(eng, passed, *waits):
            for on, value in waits:
                if type(value) is not int or value > 0:
                    eng.wait_ge(on, value)
                    eng.sem_inc(S[passed], 1)

        def run_steps(eng, step):
            step(-1, False, False, True)
            step(0, False, True, True)
            step(1, True, True, True)
            with eng.Fori(2, NB - 1) as b:
                step(b, True, True, True)
            step(NB - 1, True, True, False)
            step(NB, True, False, False)

        def run_tiles(eng, step):
            step(0, 0, False, True, False)
            step(1, 1, True, True, False)
            step(2, 0, True, True, False)
            with eng.Fori(1, NT // 2 - 1) as pair:
                step(2 * pair + 1, 1, True, True, True)
                step(2 * pair + 2, 0, True, True, True)
            step(NT - 1, 1, True, False, True)
            step(NT, 0, True, False, True)

        def half(j, odd):
            return j // 2 if type(j) is int else (j - odd) // 2

        @block.sync
        def _(sp):
            def load_batch(b):
                sp.dma_start(x_all[:, bass.ds(U * b, U), :], x_v[:, bass.ds(U * b, U), :]).then_inc(S["batch_loaded"], 16)
                sp.dma_start(ctx_all[:, bass.ds(U * b, U), :], ctx_v[:, bass.ds(U * b, U), :]).then_inc(S["batch_loaded"], 16)

            load_batch(0)
            with sp.Fori(1, NB) as b:
                sp.wait_ge(S["batch_loaded"], 32 * b)
                load_batch(b)

            sp.wait_ge(S["tables_ready"], 2)
            sp.wait_ge(S["scattered"], 16 * U * TOPK * NB)
            sp.wait_ge(S["spare_zeroed"], 16)

            def load_tile(j, s, first):
                e = sp.value_load(expert_of[0:1, bass.ds(j, 1)], min_val=0, max_val=E - 1)
                row = sp.value_load(x_row[0:1, bass.ds(j, 1)], min_val=0, max_val=SPARE)
                wait_apart(sp, "sp_passed", (S["expert_ready"], e + 1), (S["xT_done"], 0 if first else j - 1))
                sp.dma_start(xg[:, s, :], x_sorted[bass.ds(row, P), :]).then_inc(xg_loaded[s], 16)

            def store_tile(j, s):
                wait_apart(sp, "sp_passed", (S["y_evac"], j + 1))
                sp.dma_start(y_sorted[bass.ds(P * j, P), :], y_sb[:, s, :]).then_inc(y_stored[s], 16)

            load_tile(0, 0, True)
            load_tile(1, 1, True)
            with sp.Fori(1, NT // 2) as pair:
                for s in range(2):
                    load_tile(2 * pair + s, s, False)
                    store_tile(2 * pair + s - 2, s)
            for s in range(2):
                store_tile(NT - 2 + s, s)
            for g in range(NG):
                sp.wait_ge(S["combined"], TOPK * (g + 1))
                sp.dma_start(out_v[:, g, :], x_all[:, g, :]).then_inc(S["out_stored"], 16)
            sp.wait_ge(S["out_stored"], 16 * NG)

        @block.gpsimd
        def _(pool):
            pool.memset(ident[:], 0.0).then_inc(S["const_zero"], 1)
            pool.memset(mean_mat[:], 1.0 / P).then_inc(S["const_ready"], 1)
            pool.memset(eps[:], EPS).then_inc(S["const_ready"], 1)
            pool.wait_ge(S["const_zero"], 1)
            pool.affine_select(out=ident[:], in_=ident[:], compare_op=ALU.not_equal, fill=1.0, base=0,
                               pattern=[[-1, P]], channel_multiplier=1).then_inc(S["const_ready"], 1)
            pool.memset(ones_b[:], 1.0).then_inc(S["const_ready"], 1)
            pool.memset(neg_half[:], -0.5).then_inc(S["const_ready"], 1)
            pool.memset(mask_sum[:], 0.0).then_inc(S["const_ready"], 1)
            pool.memset(zero_rows[:], 0.0).then_inc(S["const_ready"], 1)
            pool.iota(rowbase_i[:], [[REGION, E]], base=0, channel_multiplier=0).then_inc(S["consts_i"], 1)
            pool.iota(lane_i[:], [[0, 1]], base=0, channel_multiplier=1).then_inc(S["consts_i"], 1)
            pool.iota(tile_no_i[:], [[1, NT]], base=0, channel_multiplier=0).then_inc(S["consts_i"], 1)
            pool.wait_ge(S["const_ready"], 7)
            pool.wait_ge(S["consts_i"], 3)
            pool.affine_select(out=tri[:], in_=ones_b[:], compare_op=ALU.is_gt, fill=0.0, base=0,
                               pattern=[[1, P]], channel_multiplier=-1).then_inc(S["consts_f"], 1)
            pool.affine_select(out=tri_incl[:], in_=ones_b[0:E, 0:E], compare_op=ALU.is_ge, fill=0.0, base=0,
                               pattern=[[1, E]], channel_multiplier=-1).then_inc(S["consts_f"], 1)
            pool.tensor_copy(rowbase[:], rowbase_i[:]).then_inc(S["consts_f"], 1)
            pool.tensor_copy(lane[:], lane_i[:]).then_inc(S["consts_f"], 1)
            pool.tensor_copy(tile_no[:], tile_no_i[:]).then_inc(S["consts_f"], 1)
            pool.dma_start(x_sorted[SPARE:SPARE + P, :], zero_rows[:]).then_inc(S["spare_zeroed"], 16)

            def load_raw(e, s):
                gate_up = w_raw[:, s, 0:GU_END].rearrange("p (c i) -> p c i", c=HC)
                pool.dma_start(gate_up[:, :, 0:I], w_gate[bass.ds(e, 1), :, :].rearrange("a (c p) i -> p (a c) i", p=P)).then_inc(raw_loaded[s], 16)
                pool.dma_start(gate_up[:, :, I:2 * I], w_up[bass.ds(e, 1), :, :].rearrange("a (c p) i -> p (a c) i", p=P)).then_inc(raw_loaded[s], 16)
                pool.dma_start(w_raw[:, s, GU_END:DA_END], w_down[bass.ds(e, 1), 0:P, :].rearrange("a p h -> (a p) h")).then_inc(raw_loaded[s], 16)
                for at in (0, I2):
                    pool.dma_start(w_raw[at:at + I2, s, DA_END:WCOLS], w_down[bass.ds(e, 1), P:I, :].rearrange("a p h -> (a p) h")).then_inc(raw_loaded[s], 16)

            load_raw(0, 0)
            load_raw(1, 1)

            def pow_rstd(var, out_, ready, n, done):
                pool.wait_ge(S[ready], n)
                pool.tensor_tensor(out_, var, neg_half[:, 0:var.shape[1]], ALU.pow).then_inc(S[done], 1)

            def add_ctx(b):
                pool.wait_ge(S["xn1_ready"], b + 1)
                pool.wait_ge(S["batch_loaded"], 32 * b + 32)
                xs = x_all[:, bass.ds(U * b, U), :]
                pool.tensor_tensor(xs, xs, ctx_all[:, bass.ds(U * b, U), :], ALU.add).then_inc(S["xc_ready"], 1)

            def scatter(b, u):
                wait_apart(pool, "pool_passed", (S["slots_ready"], b + 1))
                for k in range(TOPK):
                    pool.indirect_dma_start(out=x_sorted, out_offset=bass.IndirectOffsetOnAxis(ap=slots[:, u, k:k + 1], axis=0),
                                            in_=xn2[:, u, :], in_offset=None).then_inc(S["scattered"], 16)

            def step(b, prev, cur, nxt, old=True):
                if nxt:
                    pow_rstd(var1[:], rstd1[:], "var1_ready", b + 2, "rstd1_ready")
                if prev and old:
                    scatter(b - 2, 0)
                if prev:
                    pow_rstd(varh[:], rstdh[:], "varh_ready", b, "rstdh_ready")
                if prev and old:
                    scatter(b - 2, 1)
                if cur:
                    add_ctx(b)
                if prev:
                    pow_rstd(var2[:], rstd2[:], "var2_ready", b, "rstd2_ready")

            step(-1, False, False, True)
            step(0, False, True, True)
            step(1, True, True, True, old=False)
            with pool.Fori(2, NB - 1) as b:
                step(b, True, True, True)
            step(NB - 1, True, True, False)
            step(NB, True, False, False)
            for u in range(U):
                scatter(NB - 1, u)

            def zero_padding(e, s):
                wait_apart(pool, "pool_passed", (S["pad_zeroed"], 16 * e - 16))
                pool.tensor_copy(pad_now[s][:], pad_slot[:, bass.ds(e, 1)]).then_inc(S["pad_copied"], 1)
                wait_apart(pool, "pool_passed", (S["pad_copied"], e + 1))
                pool.indirect_dma_start(out=x_sorted, out_offset=bass.IndirectOffsetOnAxis(ap=pad_now[s][:], axis=0),
                                        in_=zero_rows[:], in_offset=None).then_inc(S["pad_zeroed"], 16)

            def split(e, s, pair, reuse, more):
                free = pool.value_load(cum_row[0:1, bass.ds(e - 2, 1)], min_val=1, max_val=NT) if reuse else 0
                wait_apart(pool, "pool_passed", (raw_loaded[s], 80 * pair + 80), (S["y_done"], free))
                pool.tensor_copy(w_hi[:, s, :], w_raw[:, s, :]).then_inc(S["hi_split"], 1)
                pool.wait_ge(S["hi_split"], e + 1)
                pool.wait_ge(S["pad_zeroed"], 16 * e + 16)
                pool.tensor_tensor(w_lo[:, s, :], w_raw[:, s, :], w_hi[:, s, :].bitcast(F32), ALU.subtract).then_inc(S["expert_ready"], 1)
                if more:
                    pool.wait_ge(S["expert_ready"], e + 1)
                    load_raw(e + 2, s)

            pool.wait_ge(S["tables_ready"], 2)
            for s in range(2):
                zero_padding(s, s)
                split(s, s, 0, False, True)
            with pool.Fori(1, E // 2 - 1) as pair:
                for s in range(2):
                    zero_padding(2 * pair + s, s)
                    split(2 * pair + s, s, pair, True, True)
            for s in range(2):
                zero_padding(E - 2 + s, s)
                split(E - 2 + s, s, E // 2 - 1, True, False)

            pool.wait_ge(y_stored[0], 16 * (NT // 2))
            pool.wait_ge(y_stored[1], 16 * (NT // 2))
            pool.wait_ge(S["y_slots_ready"], 1)
            for g in range(NG):
                if g >= 2:
                    pool.wait_ge(S["combined"], TOPK * (g - 1))
                for k in range(TOPK):
                    pool.indirect_dma_start(out=y_got[:, g % 2, k, :], out_offset=None, in_=y_sorted,
                                            in_offset=bass.IndirectOffsetOnAxis(ap=slots_all[:, g, k:k + 1], axis=0)).then_inc(y_got_loaded[g % 2], 16)

        @block.scalar
        def _(act_e):
            act_e.dma_start(raw_proj[:, 0, :], theta_w).then_inc(S["proj_loaded"], 16)
            act_e.dma_start(raw_proj[:, 1, :], phi_w).then_inc(S["proj_loaded"], 16)
            act_e.dma_start(raw_proj[:, 2, :], g_w).then_inc(S["proj_loaded"], 16)
            act_e.dma_start(raw_out, out_w.rearrange("(u p) l -> p u l", p=P)).then_inc(S["outw_loaded"], 16)
            act_e.dma_start(raw_gate, gate_w).then_inc(S["gatew_loaded"], 16)
            act_e.dma_start(th_b[:], theta_b.rearrange("(l a) -> l a", a=1)).then_inc(S["vec_loaded"], 16)
            act_e.dma_start(ph_b[:], phi_b.rearrange("(l a) -> l a", a=1)).then_inc(S["vec_loaded"], 16)
            act_e.dma_start(gb_row[:], g_b.rearrange("(a l) -> a l", a=1).to_broadcast([P, L])).then_inc(S["vec_loaded"], 16)
            with nc.allow_non_contiguous_dma(reason="256 biases, once"):
                act_e.dma_start(o_b[:], out_b.rearrange("(u p) -> p u", p=P)).then_inc(S["vec_loaded"], 16)
            act_e.dma_start(gam[:], gamma).then_inc(S["vec_loaded"], 16)
            act_e.dma_start(bet[:], beta).then_inc(S["vec_loaded"], 16)
            act_e.wait_ge(S["vec_loaded"], 16 * 6)
            act_e.wait_ge(S["const_ready"], 3)

            def step(b, prev, cur, nxt):
                if cur:
                    if prev:
                        act_e.wait_ge(S["pt_done"], TC * b)
                    for t in range(TC):
                        act_e.wait_ge(S["rowmax_ready"], TC * b + t + 1)
                        act_e.activation(prob[:, t, :], bank[t][:], ACT.Exp, bias=nmax[:, t:t + 1],
                                         accum_out=esum[:, t:t + 1]).then_inc(S["exp_ready"], 1)
                if prev:
                    act_e.wait_ge(S["hB_ready"], b)
                    wait(act_e, "outp_done", U * b - U)
                    act_e.activation(hR[:], hB[:], ACT.Relu).then_inc(S["h_ready"], 1)
                if nxt:
                    if cur:
                        act_e.wait_ge(S["scores_done"], TC * b + TC)
                    act_e.wait_ge(S["theta_done"], b + 2)
                    act_e.activation(thX[:], bank[THETA][:], ACT.Identity, bias=th_b[:]).then_inc(S["theta_ready"], 1)
                    act_e.wait_ge(S["phi_done"], b + 2)
                    act_e.activation(phX[:], bank[PHI][:], ACT.Identity, bias=ph_b[:]).then_inc(S["phi_ready"], 1)
                if cur:
                    if prev:
                        act_e.wait_ge(S["pv_done"], b)
                    for s in (0, 2):
                        act_e.wait_ge(S["pt_done"], TC * b + s + 1)
                        act_e.activation(probT[:, s, :], bank[s % 2][:], ACT.Copy).then_inc(S["pt_act"], 1)
                if prev:
                    for u in range(U):
                        act_e.wait_ge(S["xnT_done"], U * b - U + u + 1)
                        wait(act_e, "logits_done", U * b - U)
                        act_e.activation(xnTb[:, u, :, :], bank[2 + u][:].rearrange("p (c t) -> p c t", c=HC), ACT.Copy).then_inc(S["xnT_ready"], 1)
                    act_e.wait_ge(S["zl_ready"], b)
                    wait(act_e, "hit_w_ready", b - 1)
                    act_e.activation(ez[:], zl[:], ACT.Exp).then_inc(S["ez_ready"], 1)

            run_steps(act_e, step)

            def xT_hi_part(j, s, first):
                act_e.wait_ge(S["xT_done"], j + 1)
                if not first:
                    act_e.wait_ge(S["gu_done"], j - 1)
                act_e.activation(xT_hi[:, s, :], bank[s][:], ACT.Copy).then_inc(S["xT_hi_ready"], 1)

            def ffn(j, s, prev, nxt, old):
                o = 1 - s
                if prev:
                    act_e.wait_ge(S["actT_done"], j)
                    if old:
                        act_e.wait_ge(S["y_done"], j - 2)
                    act_e.activation(aA_hi[:, o, :], bank[4 + o][:, 0:P], ACT.Copy).then_inc(S["aT_hi_ready"], 1)
                    act_e.activation(aB[0:I2, o, :], bank[4 + o][0:I2, P:2 * P], ACT.Copy).then_inc(S["aB_hi_ready"], 1)
                if not (type(j) is int and j == NT):
                    act_e.wait_ge(S["gu_done"], j + 1)
                    if old:
                        act_e.wait_ge(S["act_ready"], j - 1)
                    act_e.activation(sil[:, s, :], bank[2 + s][:, 0:I], ACT.Silu).then_inc(S["sil_ready"], 1)
                if nxt:
                    xT_hi_part(j + 1, o, not prev)
                if prev:
                    act_e.wait_ge(S["y_done"], j)
                    if old:
                        act_e.wait_ge(y_stored[o], 16 * half(j - 1, o))
                    act_e.activation(y_sb[:, o, :], bank[6 + o][:], ACT.Copy).then_inc(S["y_evac"], 1)

            xT_hi_part(0, 0, True)
            run_tiles(act_e, ffn)

        @block.vector
        def _(dve):
            for k in range(3):
                dve.wait_ge(S["wT_done"], k + 1)
                dve.tensor_copy(projT[:, k, :, :], bank[k][:, 0:U * L].rearrange("p (u l) -> p u l", u=U)).then_inc(S["wT_ready"], 1)
            dve.wait_ge(S["wT_done"], 5)
            dve.tensor_copy(outT[:], bank[3][:, 0:D]).then_inc(S["wT_ready"], 1)
            dve.tensor_copy(gateT[:], bank[4][:, 0:HC * E].rearrange("p (c e) -> p c e", c=HC)).then_inc(S["wT_ready"], 1)
            dve.wait_ge(S["vec_loaded"], 16 * 6)
            dve.wait_ge(S["consts_f"], 5)

            def step(b, prev, cur, nxt):
                if nxt:
                    wait_apart(dve, "dve_passed", (S["batch_loaded"], 32 * b + 64))
                    for u in range(U):
                        dve.bn_stats(bn1[:, u, :], x_all[:, bass.ds(U * b + U + u, 1), :].rearrange("p a t -> p (a t)")).then_inc(S["bn1_done"], 1)
                    wait_apart(dve, "dve_passed", (S["bn1_done"], U * b + 2 * U))
                    for u in range(U):
                        m = dve.bn_aggr(mv1[:, u, :], bn1[:, u, :])
                    m.then_inc(S["mv1_ready"], 1)
                    dve.wait_ge(S["mv1_ready"], b + 2)
                    dve.tensor_scalar(var1[:], mv1[:, :, 1], EPS, None, ALU.add).then_inc(S["var1_ready"], 1)
                if cur:
                    for t in range(TC):
                        dve.wait_ge(S["scores_done"], TC * b + t + 1)
                        if prev:
                            dve.wait_ge(S["exp_ready"], TC * b - TC + t + 1)
                        dve.tensor_reduce(nmax[:, t:t + 1], bank[t][:], AX_X, ALU.max, negate=True).then_inc(S["rowmax_ready"], 1)
                if nxt:
                    dve.wait_ge(S["rstd1_ready"], b + 2)
                    dve.wait_ge(S["mv1_ready"], b + 2)
                    if cur:
                        dve.wait_ge(S["g_done"], b + 1)
                    for u in range(U):
                        m = dve.tensor_scalar(xn1[:, u, :], x_all[:, bass.ds(U * b + U + u, 1), :].rearrange("p a t -> p (a t)"),
                                              mv1[:, u, 0:1], rstd1[:, u:u + 1], ALU.subtract, ALU.mult)
                    m.then_inc(S["xn1_ready"], 1)
                if prev:
                    dve.wait_ge(S["mm2_done"], b)
                    dve.tensor_scalar(varh[:], bank[THETA][:, 0:1], EPS, None, ALU.add).then_inc(S["varh_ready"], 1)
                    dve.wait_ge(S["mu_ready"], b)
                    dve.scalar_tensor_tensor(hA[:], bank[ATT][:], mu[:], gam[:], ALU.subtract, ALU.mult).then_inc(S["hA_ready"], 1)
                    dve.wait_ge(S["hA_ready"], b)
                    wait(dve, "h_ready", b - 1)
                    dve.wait_ge(S["rstdh_ready"], b)
                    dve.scalar_tensor_tensor(hB[:], hA[:], rstdh[:], bet[:], ALU.mult, ALU.add).then_inc(S["hB_ready"], 1)
                if cur:
                    dve.wait_ge(S["exp_ready"], TC * b + TC)
                    dve.reciprocal(erec[:], esum[:]).then_inc(S["erec_ready"], 1)
                    dve.wait_ge(S["erec_ready"], b + 1)
                    for t in range(TC):
                        m = dve.tensor_scalar(prob[:, t, :], prob[:, t, :], erec[:, t:t + 1], None, ALU.mult)
                    m.then_inc(S["pn_ready"], 1)
                if prev:
                    dve.wait_ge(S["xc_ready"], b)
                    for u in range(U):
                        xs = x_all[:, bass.ds(U * b - U + u, 1), :].rearrange("p a t -> p (a t)")
                        dve.wait_ge(S["outp_done"], U * b - U + u + 1)
                        dve.scalar_tensor_tensor(xs, bank[THETA + u][:], o_b[:, u:u + 1], xs, ALU.add, ALU.add).then_inc(S["x2_done"], 1)
                    for u in range(U):
                        xs = x_all[:, bass.ds(U * b - U + u, 1), :].rearrange("p a t -> p (a t)")
                        wait_apart(dve, "dve_passed", (S["x2_done"], U * b - U + u + 1))
                        dve.bn_stats(bn2[:, u, :], xs).then_inc(S["bn2_done"], 1)
                    wait_apart(dve, "dve_passed", (S["bn2_done"], U * b))
                    for u in range(U):
                        m = dve.bn_aggr(mv2[:, u, :], bn2[:, u, :])
                    m.then_inc(S["mv2_ready"], 1)
                    dve.wait_ge(S["mv2_ready"], b)
                    dve.tensor_scalar(var2[:], mv2[:, :, 1], EPS, None, ALU.add).then_inc(S["var2_ready"], 1)
                if cur:
                    for s in (1, 3):
                        dve.wait_ge(S["pt_done"], TC * b + s + 1)
                        dve.tensor_copy(probT[:, s, :], bank[s % 2][:]).then_inc(S["pt_dve"], 1)
                if prev:
                    dve.wait_ge(S["rstd2_ready"], b)
                    wait(dve, "scattered", 16 * U * TOPK * (b - 1))
                    for u in range(U):
                        xs = x_all[:, bass.ds(U * b - U + u, 1), :].rearrange("p a t -> p (a t)")
                        dve.tensor_scalar(xn2[:, u, :], xs, mv2[:, u, 0:1], rstd2[:, u:u + 1], ALU.subtract, ALU.mult).then_inc(S["xn2_ready"], 1)
                    lg = bank[THETA][:, 0:U * E].rearrange("p (u e) -> p u e", u=U)
                    wait_apart(dve, "dve_passed", (S["logits_done"], U * b))
                    for u in range(U):
                        m = dve.max(top8[:, u, :], lg[:, u, :])
                    m.then_inc(S["top8_ready"], 1)
                    dve.wait_ge(S["top8_ready"], b)
                    dve.tensor_tensor(zl[:], lg, top8[:, :, 0:1].to_broadcast([P, U, E]), ALU.subtract).then_inc(S["zl_ready"], 1)
                    for u in range(U):
                        m = dve.match_replace(repl[:, u, :], top8[:, u, :], lg[:, u, :], LOWEST)
                    m.then_inc(S["repl_ready"], 1)
                    dve.wait_ge(S["repl_ready"], b)
                    dve.tensor_tensor(mask[:], repl[:], lg, ALU.is_lt).then_inc(S["mask_ready"], 1)
                    dve.wait_ge(S["pos_done"], b)
                    dve.tensor_tensor(key0[:], bank[THETA][:, 2 * U * E:3 * U * E].rearrange("p (u e) -> p u e", u=U),
                                      rowbase[:].rearrange("p (a e) -> p a e", a=1).to_broadcast([P, U, E]), ALU.add).then_inc(S["key0_ready"], 1)
                    dve.tensor_tensor(mask_sum[:], mask_sum[:], mask[:, 0, :], ALU.add).then_inc(S["mask0_added"], 1)
                    dve.wait_ge(S["key0_ready"], b)
                    dve.scalar_tensor_tensor(key[:], key0[:], 1.0, mask[:], ALU.add, ALU.mult).then_inc(S["key_ready"], 1)
                    dve.wait_ge(S["mask0_added"], b)
                    dve.tensor_tensor(mask_sum[:], mask_sum[:], mask[:, 1, :], ALU.add).then_inc(S["mask_sum_ready"], 1)
                    wait_apart(dve, "dve_passed", (S["key_ready"], b))
                    for u in range(U):
                        m = dve.max(key8[:, u, :], key[:, u, :])
                    m.then_inc(S["key8_ready"], 1)
                    dve.wait_ge(S["key8_ready"], b)
                    dve.tensor_scalar(slots[:], key8[:], -1.0, None, ALU.add).then_inc(S["slots_ready"], 1)
                    dve.tensor_copy(key_all[:, bass.ds(U * b - U, U), :], key[:])
                    dve.tensor_tensor(hit[:], key[:].rearrange("p u (a e) -> p u a e", a=1).to_broadcast([P, U, TOPK, E]),
                                      key8[:].rearrange("p u (k a) -> p u k a", a=1).to_broadcast([P, U, TOPK, E]), ALU.is_equal).then_inc(S["hit_ready"], 1)
                    dve.wait_ge(S["hit_ready"], b)
                    dve.wait_ge(S["ez_ready"], b)
                    dve.tensor_tensor(hit_w[:], hit[:], ez[:].rearrange("p u (a e) -> p u a e", a=1).to_broadcast([P, U, TOPK, E]),
                                      ALU.mult).then_inc(S["hit_w_ready"], 1)
                    dve.wait_ge(S["hit_w_ready"], b)
                    dve.tensor_reduce(wk[:], hit_w[:], AX_X, ALU.add).then_inc(S["wk_ready"], 1)
                    dve.wait_ge(S["wk_ready"], b)
                    dve.tensor_reduce(wsum[:], wk[:], AX_X, ALU.add).then_inc(S["wsum_ready"], 1)
                    dve.wait_ge(S["wsum_ready"], b)
                    dve.reciprocal(wrec[:], wsum[:]).then_inc(S["wrec_ready"], 1)
                    dve.wait_ge(S["wrec_ready"], b)
                    dve.tensor_tensor(wk_all[:, bass.ds(U * b - U, U), :], wk[:],
                                      wrec[:].rearrange("p (u a) -> p u a", a=1).to_broadcast([P, U, TOPK]), ALU.mult).then_inc(S["w_ready"], 1)
                if cur:
                    dve.wait_ge(S["pv_done"], b + 1)
                    dve.bn_stats(bnO[:], bank[ATT][:]).then_inc(S["bnO_done"], 1)
                    wait_apart(dve, "dve_passed", (S["bnO_done"], b + 1))
                    dve.bn_aggr(mvO[:], bnO[:]).then_inc(S["bnO_ready"], 1)
                if nxt:
                    dve.wait_ge(S["g_done"], b + 2)
                    dve.tensor_tensor(gX[:], bank[GPROJ][:].rearrange("p (s l) -> p s l", s=TC),
                                      gb_row[:].rearrange("p (a l) -> p a l", a=1).to_broadcast([P, TC, L]), ALU.add).then_inc(S["gx_ready"], 1)
                if cur:
                    dve.wait_ge(S["mm1_done"], b + 1)
                    dve.wait_ge(S["bnO_ready"], b + 1)
                    dve.tensor_copy(mu[:], bank[PHI][:, 0:1]).then_inc(S["mu_ready"], 1)
                    dve.wait_ge(S["mu_ready"], b + 1)
                    dve.tensor_tensor(dmu[:], mvO[:, 0:1], mu[:], ALU.subtract).then_inc(S["dmu_ready"], 1)
                    dve.wait_ge(S["dmu_ready"], b + 1)
                    dve.scalar_tensor_tensor(vO[:], dmu[:], dmu[:], mvO[:, 1:2], ALU.mult, ALU.add).then_inc(S["v_ready"], 1)

            run_steps(dve, step)
            dve.wait_ge(S["w_ready"], NB)

            dve.wait_ge(S["count_done"], 2)
            dve.scalar_tensor_tensor(pad_slot[:], bank[0][:, 0:E], lane[:], rowbase[:], ALU.add, ALU.add).then_inc(S["tables_ready"], 1)
            dve.tensor_copy(n_col[:], bank[1][0:E, 0:1]).then_inc(S["n_col_ready"], 1)
            dve.wait_ge(S["n_col_ready"], 1)
            dve.tensor_scalar(n_cmp[:], tile_no[:, 0:TOK // P], float(P), n_col[:], ALU.mult, ALU.is_lt).then_inc(S["n_cmp_ready"], 1)
            dve.wait_ge(S["n_cmp_ready"], 1)
            dve.tensor_reduce(n_tile0[:], n_cmp[:], AX_X, ALU.add).then_inc(S["n_tile0_ready"], 1)
            dve.wait_ge(S["n_tile0_ready"], 1)
            dve.tensor_scalar(n_tile[:], n_tile0[:], 1.0, None, ALU.max).then_inc(S["n_tile_ready"], 1)
            dve.tensor_scalar(n_tile_b[:], ones_b[0:E, :], n_tile0[:], 1.0, ALU.mult, ALU.max).then_inc(S["n_tile_ready"], 1)
            dve.wait_ge(S["cum_done"], 1)
            dve.tensor_copy(cum_col[:], bank[2][0:E, 0:1]).then_inc(S["cum_ready"], 1)
            dve.tensor_copy(cum_row[:], bank[3][0:1, 0:E]).then_inc(S["cum_ready"], 1)
            dve.wait_ge(S["cum_ready"], 2)
            dve.tensor_scalar(past[:], tile_no[:], cum_col[:], None, ALU.is_ge).then_inc(S["past_ready"], 1)
            dve.wait_ge(S["owner_done"], 1)
            dve.tensor_copy(owner[:], bank[4][0:1, 0:NT]).then_inc(S["owner_ready"], 1)
            dve.tensor_scalar(owner_row[:], bank[4][0:1, 0:NT], float(REGION), None, ALU.mult).then_inc(S["owner_ready"], 1)
            dve.tensor_tensor(tile_in[:], tile_no[0:1, :], bank[5][0:1, 0:NT], ALU.subtract).then_inc(S["owner_ready"], 1)
            dve.wait_ge(S["owner_ready"], 3)
            dve.tensor_scalar(expert_of[:], owner[:], float(E - 1), None, ALU.min).then_inc(S["owner_ready"], 1)
            dve.scalar_tensor_tensor(row_f[:], tile_in[:], float(P), owner_row[:], ALU.mult, ALU.add).then_inc(S["row_f_ready"], 1)
            dve.wait_ge(S["owner_ready"], 4)
            dve.tensor_scalar(half_of[:], expert_of[:], 1, None, ALU.bitwise_and)
            dve.wait_ge(S["row_f_ready"], 1)
            dve.tensor_scalar(x_row[:], row_f[:], float(SPARE), None, ALU.min).then_inc(S["tables_ready"], 1)

            def xT_lo_part(j, s, first):
                dve.wait_ge(S["xT_hi_ready"], j + 1)
                if not first:
                    dve.wait_ge(S["gu_done"], j - 1)
                dve.tensor_tensor(xT_lo[:, s, :], bank[s][:], xT_hi[:, s, :].bitcast(F32), ALU.subtract).then_inc(S["xT_lo_ready"], 1)

            def ffn(j, s, prev, nxt, old):
                o = 1 - s
                if prev:
                    dve.wait_ge(S["aT_hi_ready"], j)
                    if old:
                        dve.wait_ge(S["y_done"], j - 2)
                    dve.wait_ge(S["aB_hi_ready"], j)
                    dve.tensor_tensor(aA_lo[:, o, :], bank[4 + o][:, 0:P], aA_hi[:, o, :].bitcast(F32), ALU.subtract)
                    dve.tensor_tensor(aB[I2:2 * I2, o, :], bank[4 + o][0:I2, P:2 * P], aB[0:I2, o, :].bitcast(F32), ALU.subtract).then_inc(S["aT_lo_ready"], 1)
                if not (type(j) is int and j == NT):
                    dve.wait_ge(S["sil_ready"], j + 1)
                    if old:
                        dve.wait_ge(S["actT_done"], j - 1)
                    dve.tensor_tensor(act[:, s, :], sil[:, s, :], bank[2 + s][:, I:2 * I], ALU.mult).then_inc(S["act_ready"], 1)
                if nxt:
                    xT_lo_part(j + 1, o, not prev)

            dve.wait_ge(S["before_done"], 1)
            dve.scalar_tensor_tensor(delta[:], bank[6][:, 0:E], float(P), rowbase[:], ALU.mult, ALU.subtract).then_inc(S["delta_ready"], 1)
            dve.wait_ge(S["delta_ready"], 1)
            dve.tensor_tensor(key_all[:], key_all[:], delta[:].rearrange("p (a e) -> p a e", a=1).to_broadcast([P, NG, E]), ALU.add).then_inc(S["y_key_ready"], 1)
            dve.wait_ge(S["y_key_ready"], 1)
            for g in range(NG):
                m = dve.max(y_key8[:, g, :], key_all[:, g, :])
            m.then_inc(S["y_key8_ready"], 1)
            dve.wait_ge(S["y_key8_ready"], 1)
            dve.tensor_scalar(slots_all[:], y_key8[:], -1.0, None, ALU.add).then_inc(S["y_slots_ready"], 1)

            xT_lo_part(0, 0, True)
            run_tiles(dve, ffn)
            for g in range(NG):
                dve.wait_ge(y_got_loaded[g % 2], 16 * TOPK * (g // 2 + 1))
                for k in range(TOPK):
                    if k:
                        dve.wait_ge(S["combined"], TOPK * g + k)
                    dve.scalar_tensor_tensor(x_all[:, g, :], y_got[:, g % 2, k, :], wk_all[:, g, k:k + 1], x_all[:, g, :],
                                             ALU.mult, ALU.add).then_inc(S["combined"], 1)

        @block.tensor
        def _(pe):
            pe.wait_ge(S["const_ready"], 7)
            pe.wait_ge(S["consts_f"], 5)
            pe.wait_ge(S["proj_loaded"], 48)
            for k in range(3):
                for u in range(U):
                    m = pe.transpose(bank[k][:, u * L:(u + 1) * L], raw_proj[:, k, u * P:(u + 1) * P], ident[:])
                m.then_inc(S["wT_done"], 1)
            pe.wait_ge(S["outw_loaded"], 16)
            for u in range(U):
                m = pe.transpose(bank[3][:, u * P:(u + 1) * P], raw_out[:, u, :], ident[:])
            m.then_inc(S["wT_done"], 1)
            pe.wait_ge(S["gatew_loaded"], 16)
            for c in range(HC):
                m = pe.transpose(bank[4][:, c * E:(c + 1) * E], raw_gate[:, c * P:(c + 1) * P], ident[0:E, 0:E])
            m.then_inc(S["wT_done"], 1)
            pe.wait_ge(S["wT_ready"], 5)

            def step(b, prev, cur, nxt):
                if cur:
                    pe.wait_ge(S["theta_ready"], b + 1)
                    pe.wait_ge(S["phi_ready"], b + 1)
                    if prev:
                        wait(pe, "pt_act", 2 * b)
                        wait(pe, "pt_dve", 2 * b)
                        wait(pe, "xnT_ready", U * b - U)
                    for t in range(TC):
                        pe.matmul(bank[t][:], thX[:, t * P:(t + 1) * P], phX[:], start=True, stop=True).then_inc(S["scores_done"], 1)
                if prev:
                    pe.wait_ge(S["v_ready"], b)
                    wait(pe, "key0_ready", b - 1)
                    pe.matmul(bank[THETA][:, 0:1], mean_mat[:], vO[:], start=True, stop=True).then_inc(S["mm2_done"], 1)
                if nxt:
                    pe.wait_ge(S["xn1_ready"], b + 2)
                    pe.wait_ge(S["batch_loaded"], 32 * b + 64)
                    if prev:
                        pe.wait_ge(S["varh_ready"], b)
                    for u in range(U):
                        m = pe.matmul(bank[THETA][:], projT[:, 0, u, :], ctx_all[:, bass.ds(U * b + U + u, 1), :].rearrange("p a t -> p (a t)"),
                                      start=(u == 0), stop=(u == U - 1))
                    m.then_inc(S["theta_done"], 1)
                    for u in range(U):
                        m = pe.matmul(bank[PHI][:], projT[:, 1, u, :], xn1[:, u, :], start=(u == 0), stop=(u == U - 1))
                    m.then_inc(S["phi_done"], 1)
                    if cur:
                        pe.wait_ge(S["gx_ready"], b + 1)
                    for s in range(TC):
                        for u in range(U):
                            m = pe.matmul(bank[GPROJ][:, s * L:(s + 1) * L], xn1[:, u, s * P:(s + 1) * P], projT[:, 2, u, :],
                                          start=(u == 0), stop=(u == U - 1))
                    m.then_inc(S["g_done"], 1)
                if prev:
                    pe.wait_ge(S["h_ready"], b)
                    if nxt:
                        pe.wait_ge(S["theta_ready"], b + 2)
                        pe.wait_ge(S["phi_ready"], b + 2)
                    else:
                        pe.wait_ge(S["varh_ready"], b)
                    for u in range(U):
                        pe.matmul(bank[THETA + u][:], outT[:, u * P:(u + 1) * P], hR[:], start=True, stop=True).then_inc(S["outp_done"], 1)
                if cur:
                    pe.wait_ge(S["pn_ready"], b + 1)
                    pe.wait_ge(S["gx_ready"], b + 1)

                    def pv(s):
                        pe.wait_ge(S["pt_act" if s % 2 == 0 else "pt_dve"], 2 * b + s // 2 + 1)
                        return pe.matmul(bank[ATT][:], gX[:, s, :], probT[:, s, :], start=(s == 0), stop=(s == TC - 1))

                    for s in range(TC):
                        if s >= 2:
                            pe.wait_ge(S["pt_act" if s % 2 == 0 else "pt_dve"], 2 * b + (s - 2) // 2 + 1)
                        for t in range(TC):
                            m = pe.transpose(bank[s % 2][:, t * P:(t + 1) * P], prob[:, t, s * P:(s + 1) * P], ident[:])
                        m.then_inc(S["pt_done"], 1)
                        if s >= 1:
                            pv(s - 1)
                    pv(TC - 1).then_inc(S["pv_done"], 1)
                if prev:
                    for u in range(U):
                        pe.wait_ge(S["xn2_ready"], U * b - U + u + 1)
                        for c in range(HC):
                            m = pe.transpose(bank[2 + u][:, c * P:(c + 1) * P], xn2[:, u, c * P:(c + 1) * P], ident[:])
                        m.then_inc(S["xnT_done"], 1)
                    for u in range(U):
                        pe.wait_ge(S["xnT_ready"], U * b - U + u + 1)
                        for c in range(HC):
                            m = pe.matmul(bank[THETA][:, u * E:(u + 1) * E], xnTb[:, u, c, :],
                                          gateT[:, c, :], start=(c == 0), stop=(c == HC - 1))
                        m.then_inc(S["logits_done"], 1)
                    pe.wait_ge(S["mask_ready"], b)
                    wait(pe, "mask_sum_ready", b - 1)
                    for u in range(U):
                        pos = bank[THETA][:, (2 * U + u) * E:(2 * U + u + 1) * E]
                        pe.matmul(pos, ones_b[:], mask_sum[:], start=True, stop=False)
                        if u:
                            pe.matmul(pos, ones_b[:], mask[:, 0, :], start=False, stop=False)
                        m = pe.matmul(pos, tri[:], mask[:, u, :], start=False, stop=True)
                    m.then_inc(S["pos_done"], 1)
                if cur:
                    pe.wait_ge(S["bnO_ready"], b + 1)
                    pe.matmul(bank[PHI][:, 0:1], mean_mat[:], mvO[:, 0:1], start=True, stop=True).then_inc(S["mm1_done"], 1)

            run_steps(pe, step)
            pe.wait_ge(S["mask_sum_ready"], NB)
            pe.matmul(bank[0][:, 0:E], ones_b[:], mask_sum[:], start=True, stop=True).then_inc(S["count_done"], 1)
            pe.matmul(bank[1][0:E, 0:1], mask_sum[:], ones_b[:, 0:1], start=True, stop=True).then_inc(S["count_done"], 1)
            pe.wait_ge(S["n_tile_ready"], 2)
            pe.matmul(bank[2][0:E, 0:1], tri_incl[:], n_tile[:], start=True, stop=True)
            pe.matmul(bank[3][0:1, 0:E], n_tile[:], tri_incl[:], start=True, stop=True).then_inc(S["cum_done"], 1)
            pe.wait_ge(S["past_ready"], 1)
            pe.wait_ge(S["key0_ready"], NB)
            pe.matmul(bank[4][0:1, 0:NT], ones_b[0:E, 0:1], past[:], start=True, stop=True)
            pe.matmul(bank[5][0:1, 0:NT], n_tile[:], past[:], start=True, stop=True).then_inc(S["owner_done"], 1)
            pe.matmul(bank[6][:, 0:E], n_tile_b[:], tri[0:E, 0:E], start=True, stop=True).then_inc(S["before_done"], 1)
            pe.wait_ge(S["tables_ready"], 2)

            def transpose_x(j, s, pair, first):
                pe.wait_ge(xg_loaded[s], 16 * pair + 16)
                if not first:
                    pe.wait_ge(S["xT_lo_ready"], j - 1)
                for c in range(HC):
                    m = pe.transpose(bank[s][:, c * P:(c + 1) * P], xg[:, s, c * P:(c + 1) * P], ident[:])
                m.then_inc(S["xT_done"], 1)

            def ffn(j, s, prev, nxt, old):
                o = 1 - s
                if prev:
                    pe.wait_ge(S["act_ready"], j)
                    if old:
                        pe.wait_ge(S["aT_lo_ready"], j - 2)
                    pe.transpose(bank[4 + o][:, 0:P], act[:, o, 0:P], ident[:])
                    pe.transpose(bank[4 + o][0:I2, P:2 * P], act[:, o, P:I], ident[:]).then_inc(S["actT_done"], 1)
                if not (type(j) is int and j == NT):
                    e = pe.value_load(expert_of[0:1, bass.ds(j, 1)], min_val=0, max_val=E - 1)
                    h = pe.value_load(half_of[0:1, bass.ds(j, 1)], min_val=0, max_val=1)
                    pe.wait_ge(S["expert_ready"], e + 1)
                    pe.wait_ge(S["xT_hi_ready"], j + 1)
                    if old:
                        pe.wait_ge(S["act_ready"], j - 1)
                    out_gu = bank[2 + s][:, 0:2 * I]

                    def gate_up(w, c):
                        return w[:, bass.ds(h, 1), c * 2 * I:(c + 1) * 2 * I].rearrange("p a i -> p (a i)")

                    for c in range(HC):
                        pe.matmul(out_gu, xT_hi[:, s, c * P:(c + 1) * P], gate_up(w_hi, c), start=(c == 0), stop=False)
                        pe.matmul(out_gu, xT_hi[:, s, c * P:(c + 1) * P], gate_up(w_lo, c), start=False, stop=False)
                    pe.wait_ge(S["xT_lo_ready"], j + 1)
                    for c in range(HC):
                        m = pe.matmul(out_gu, xT_lo[:, s, c * P:(c + 1) * P], gate_up(w_hi, c), start=False, stop=(c == HC - 1))
                    m.then_inc(S["gu_done"], 1)
                if nxt:
                    transpose_x(j + 1, o, half(j + 1, o), not prev)
                if prev:
                    h = pe.value_load(half_of[0:1, bass.ds(j - 1, 1)], min_val=0, max_val=1)
                    pe.wait_ge(S["aT_hi_ready"], j)
                    pe.wait_ge(S["aT_lo_ready"], j)
                    if old:
                        pe.wait_ge(S["y_evac"], j - 2)

                    def down(w, rows, lo, hi):
                        return w[0:rows, bass.ds(h, 1), lo:hi].rearrange("p a i -> p (a i)")

                    out_y = bank[6 + o][:]
                    pe.matmul(out_y, aA_hi[:, o, :], down(w_hi, P, GU_END, DA_END), start=True, stop=False)
                    pe.matmul(out_y, aA_hi[:, o, :], down(w_lo, P, GU_END, DA_END), start=False, stop=False)
                    pe.matmul(out_y, aB[0:I2, o, :], down(w_lo, I2, DA_END, WCOLS), start=False, stop=False)
                    pe.matmul(out_y, aA_lo[:, o, :], down(w_hi, P, GU_END, DA_END), start=False, stop=False)
                    pe.matmul(out_y, aB[:, o, :], down(w_hi, P, DA_END, WCOLS), start=False, stop=True).then_inc(S["y_done"], 1)

            transpose_x(0, 0, 0, True)
            run_tiles(pe, ffn)


_INS = ['x', 'ctx_2048', 'L0_xattn_theta_w', 'L0_xattn_theta_b', 'L0_xattn_phi_w', 'L0_xattn_phi_b', 'L0_xattn_g_w', 'L0_xattn_g_b',
        'L0_xattn_ln_gamma', 'L0_xattn_ln_beta', 'L0_xattn_out_w', 'L0_xattn_out_b', 'L0_ffn_gate_w', 'L0_ffn_w_gate', 'L0_ffn_w_up',
        'L0_ffn_w_down']
_OUTS = [((8, 256, 512), 'float32')]


def kernel(**inputs):
    import numpy as _np
    import concourse.bacc as _bacc
    from concourse import mybir as _mybir
    from concourse.bass_utils import run_bass_kernel_spmd as _run

    nc = _bacc.Bacc("TRN2", target_bir_lowering=False, num_devices=1)
    arrays, args = {}, []
    for name in _INS:
        a = _np.ascontiguousarray(inputs[name])
        arrays[f"in_{name}_dram"] = a
        args.append(nc.dram_tensor(f"in_{name}_dram", a.shape, _mybir.dt.from_np(a.dtype), kind="ExternalInput").ap())
    for i, (shape, dtype) in enumerate(_OUTS):
        dt = _mybir.dt.from_np(_np.dtype(dtype))
        args.append(nc.dram_tensor(f"out_{i}_dram", shape, dt, kind="ExternalOutput").ap())
    build(nc, *args)
    r = _run(nc, [arrays], core_ids=[0])
    got = tuple(r.results[0][f"out_{i}_dram"] for i in range(len(_OUTS)))
    return got[0]
```
